# Optimizing a Trainium2 kernel written in Bass

```python
import numpy as np
import jax
import jax.numpy as jnp

def _softmax(x, axis=-1):
    return jax.nn.softmax(x, axis=axis)

def _gelu(x):
    return jax.nn.gelu(x, approximate=True)

def _silu(x):
    return jax.nn.silu(x)

def _sigmoid(x):
    return jax.nn.sigmoid(x)

def _layernorm(x, axis=-1, eps=1e-05):
    m = jnp.mean(x, axis=axis, keepdims=True)
    v = jnp.var(x, axis=axis, keepdims=True)
    return (x - m) / jnp.sqrt(v + eps)

def _scatter_add(tgt, idx, src, axis=0):
    return tgt.at[idx].add(src)

def _segment_sum(src, seg, n):
    return jax.ops.segment_sum(src, seg, n)
kernel_name = 'mk_flamingo_gated_d1_seqx_r4_5b9086'

def setup_inputs(seed: int=0):
    np.random.seed(seed)
    _w = jnp.asarray

    def _rec_inputs():
        import jax
        import jax.numpy as jnp
        _rk = jax.random.key(seed)
        x = 4.136e-05 + 0.9999 * jax.random.normal(jax.random.fold_in(_rk, 1), (4, 512, 256), jnp.float32)
        _lenS = 512 - jax.random.randint(jax.random.fold_in(_rk, 7), (4,), 0, max(1, 512 // 4) + 1, jnp.int32)
        _lenS2 = 512 - jax.random.randint(jax.random.fold_in(_rk, 8), (4,), 0, max(1, 512 // 4) + 1, jnp.int32)
        _ctx_1024P = jax.random.normal(jax.random.fold_in(_rk, 11), (4, 16, 256), jnp.float32)
        _ctx_1024c = jax.random.dirichlet(jax.random.fold_in(_rk, 511), 0.3 * jnp.ones((16,), jnp.float32), (4, 512))
        _ctx_1024t = jnp.einsum('bsk,bkd->bsd', _ctx_1024c, _ctx_1024P)
        _ctx_1024t = _ctx_1024t * jax.lax.rsqrt(jnp.mean(jnp.square(_ctx_1024t)) + 1e-12) * 0.953939
        ctx_1024 = 7.22013e-05 + 1.00017 * (_ctx_1024t + 0.3 * jax.random.normal(jax.random.fold_in(_rk, 611), (4, 512, 256), jnp.float32))
        _g = jax.random.normal(jax.random.fold_in(_rk, 9001), (2, 1), jnp.float32)
        _g = jnp.sign(_g) * jnp.maximum(jnp.abs(_g), 1.0) + (_g == 0) * 1.0
        g_xattn = _g[0]
        g_ffn = _g[1]
        return (x, ctx_1024, g_xattn, g_ffn)
    x, ctx_1024, g_xattn, g_ffn = _rec_inputs()

    def _L0_xattn_setup():
        import jax, jax.numpy as jnp
        import numpy as np
        B, L_Q, L_KV, D, H = (4, 512, 512, 256, 16)
        key = jax.random.key(seed)
        ks = jax.random.split(key, 11)
        s = 0.02
        return {'kv': jax.random.normal(ks[0], (B, L_KV, D), dtype=jnp.float32), 'q': jax.random.normal(ks[1], (B, L_Q, D), dtype=jnp.float32), 'Wq': jax.random.normal(ks[2], (D, D), dtype=jnp.float32) * s, 'bq': jnp.zeros((D,), dtype=jnp.float32), 'Wk': jax.random.normal(ks[3], (D, D), dtype=jnp.float32) * s, 'bk': jnp.zeros((D,), dtype=jnp.float32), 'Wv': jax.random.normal(ks[4], (D, D), dtype=jnp.float32) * s, 'bv': jnp.zeros((D,), dtype=jnp.float32), 'Wo': jax.random.normal(ks[5], (D, D), dtype=jnp.float32) * s, 'bo': jnp.zeros((D,), dtype=jnp.float32)}
    _L0_xattn_all = _L0_xattn_setup()
    _L0_xattn_in = {k: v for k, v in _L0_xattn_all.items() if k in ('Wq', 'bq', 'Wk', 'bk', 'Wv', 'bv', 'Wo', 'bo')}
    del _L0_xattn_all

    def _L0_ffn_setup():
        import jax, jax.numpy as jnp
        import numpy as np
        LATENT = 256
        LEAF_W = 64
        DEPTH = 4
        N_LEAVES = 2 ** DEPTH
        N_NODES = 2 ** DEPTH - 1
        B, S = (4, 512)

        def _fff_params(key, prefix):
            ks = jax.random.split(key, 4)
            d, h, l, n = (LATENT, LEAF_W, N_LEAVES, N_NODES)
            s_in = 1.0 / np.sqrt(d).astype(np.float32)
            s_h = 1.0 / np.sqrt(h).astype(np.float32)
            return {f'{prefix}_node_w': jax.random.normal(ks[0], (n, d), jnp.float32) * s_in, f'{prefix}_node_b': jax.random.normal(ks[1], (n,), jnp.float32) * s_in, f'{prefix}_w1': jax.random.normal(ks[2], (l, d, h), jnp.float32) * s_in, f'{prefix}_b1': jnp.zeros((l, h), jnp.float32), f'{prefix}_w2': jax.random.normal(ks[3], (l, h, d), jnp.float32) * s_h, f'{prefix}_b2': jnp.zeros((l, d), jnp.float32)}

        def _fff(x, node_w, node_b, w1, b1, w2, b2):
            Bx, Sx, D = x.shape
            xf = x.reshape(-1, D)
            N = xf.shape[0]
            cur = jnp.zeros((N,), jnp.int32)
            for _ in range(DEPTH):
                pw = node_w[cur]
                score = jnp.einsum('nd,nd->n', xf, pw) + node_b[cur]
                cur = 2 * cur + 1 + (score >= 0).astype(jnp.int32)
            leaf = cur - N_NODES
            sel = jax.nn.one_hot(leaf, N_LEAVES, dtype=xf.dtype)
            hidden_all = jax.nn.relu(jnp.einsum('nd,ldh->lnh', xf, w1) + b1[:, None, :])
            hidden = hidden_all * sel.T[:, :, None]
            out = jnp.einsum('lnh,lho->no', hidden, w2) + sel @ b2
            return out.reshape(Bx, Sx, D)
        key = jax.random.key(seed)
        kx, kq, kk, kv = jax.random.split(key, 4)
        inp = {'x': jax.random.normal(kx, (B, S, LATENT), jnp.float32)}
        inp.update(_fff_params(kq, 'q'))
        inp.update(_fff_params(kk, 'k'))
        inp.update(_fff_params(kv, 'v'))
        return inp
    _L0_ffn_all = _L0_ffn_setup()
    _L0_ffn_in = {k: v for k, v in _L0_ffn_all.items() if k in ('q_node_w', 'q_node_b', 'q_w1', 'q_b1', 'q_w2', 'q_b2', 'k_node_w', 'k_node_b', 'k_w1', 'k_b1', 'k_w2', 'k_b2', 'v_node_w', 'v_node_b', 'v_w1', 'v_b1', 'v_w2', 'v_b2')}
    del _L0_ffn_all
    return {'x': x, 'ctx_1024': ctx_1024, 'g_xattn': g_xattn, 'g_ffn': g_ffn, 'L0_xattn_Wq': _L0_xattn_in['Wq'], 'L0_xattn_bq': _L0_xattn_in['bq'], 'L0_xattn_Wk': _L0_xattn_in['Wk'], 'L0_xattn_bk': _L0_xattn_in['bk'], 'L0_xattn_Wv': _L0_xattn_in['Wv'], 'L0_xattn_bv': _L0_xattn_in['bv'], 'L0_xattn_Wo': _L0_xattn_in['Wo'], 'L0_xattn_bo': _L0_xattn_in['bo'], 'L0_ffn_q_node_w': _L0_ffn_in['q_node_w'], 'L0_ffn_q_node_b': _L0_ffn_in['q_node_b'], 'L0_ffn_q_w1': _L0_ffn_in['q_w1'], 'L0_ffn_q_b1': _L0_ffn_in['q_b1'], 'L0_ffn_q_w2': _L0_ffn_in['q_w2'], 'L0_ffn_q_b2': _L0_ffn_in['q_b2'], 'L0_ffn_k_node_w': _L0_ffn_in['k_node_w'], 'L0_ffn_k_node_b': _L0_ffn_in['k_node_b'], 'L0_ffn_k_w1': _L0_ffn_in['k_w1'], 'L0_ffn_k_b1': _L0_ffn_in['k_b1'], 'L0_ffn_k_w2': _L0_ffn_in['k_w2'], 'L0_ffn_k_b2': _L0_ffn_in['k_b2'], 'L0_ffn_v_node_w': _L0_ffn_in['v_node_w'], 'L0_ffn_v_node_b': _L0_ffn_in['v_node_b'], 'L0_ffn_v_w1': _L0_ffn_in['v_w1'], 'L0_ffn_v_b1': _L0_ffn_in['v_b1'], 'L0_ffn_v_w2': _L0_ffn_in['v_w2'], 'L0_ffn_v_b2': _L0_ffn_in['v_b2']}

def reference(x, ctx_1024, g_xattn, g_ffn, L0_xattn_Wq, L0_xattn_bq, L0_xattn_Wk, L0_xattn_bk, L0_xattn_Wv, L0_xattn_bv, L0_xattn_Wo, L0_xattn_bo, L0_ffn_q_node_w, L0_ffn_q_node_b, L0_ffn_q_w1, L0_ffn_q_b1, L0_ffn_q_w2, L0_ffn_q_b2, L0_ffn_k_node_w, L0_ffn_k_node_b, L0_ffn_k_w1, L0_ffn_k_b1, L0_ffn_k_w2, L0_ffn_k_b2, L0_ffn_v_node_w, L0_ffn_v_node_b, L0_ffn_v_w1, L0_ffn_v_b1, L0_ffn_v_w2, L0_ffn_v_b2):
    import jax
    import jax.numpy as jnp

    def _L0_xattn_ref(kv, q, Wq, bq, Wk, bk, Wv, bv, Wo, bo):
        import jax, jax.numpy as jnp
        import numpy as np
        B, L_Q, L_KV, D, H = (4, 512, 512, 256, 16)
        Bb, Lkv, Dm = kv.shape
        Lq = q.shape[1]
        hd = Dm // H
        scale = hd ** (-0.5)
        qh = (q @ Wq.T + bq).reshape(Bb, Lq, H, hd).transpose(0, 2, 1, 3)
        kh = (kv @ Wk.T + bk).reshape(Bb, Lkv, H, hd).transpose(0, 2, 1, 3)
        vh = (kv @ Wv.T + bv).reshape(Bb, Lkv, H, hd).transpose(0, 2, 1, 3)
        scores = jnp.einsum('bhqd,bhkd->bhqk', qh, kh) * scale
        mask = jnp.arange(Lkv)[None, :] <= jnp.arange(Lq)[:, None]
        scores = jnp.where(mask[None, None], scores, -jnp.inf)
        attn = jax.nn.softmax(scores, axis=-1)
        out = jnp.einsum('bhqk,bhkd->bhqd', attn, vh)
        out = out.transpose(0, 2, 1, 3).reshape(Bb, Lq, Dm)
        return out @ Wo.T + bo

    def _L0_ffn_ref(x, q_node_w, q_node_b, q_w1, q_b1, q_w2, q_b2, k_node_w, k_node_b, k_w1, k_b1, k_w2, k_b2, v_node_w, v_node_b, v_w1, v_b1, v_w2, v_b2):
        import jax, jax.numpy as jnp
        import numpy as np
        LATENT = 256
        LEAF_W = 64
        DEPTH = 4
        N_LEAVES = 2 ** DEPTH
        N_NODES = 2 ** DEPTH - 1
        B, S = (4, 512)

        def _fff_params(key, prefix):
            ks = jax.random.split(key, 4)
            d, h, l, n = (LATENT, LEAF_W, N_LEAVES, N_NODES)
            s_in = 1.0 / np.sqrt(d).astype(np.float32)
            s_h = 1.0 / np.sqrt(h).astype(np.float32)
            return {f'{prefix}_node_w': jax.random.normal(ks[0], (n, d), jnp.float32) * s_in, f'{prefix}_node_b': jax.random.normal(ks[1], (n,), jnp.float32) * s_in, f'{prefix}_w1': jax.random.normal(ks[2], (l, d, h), jnp.float32) * s_in, f'{prefix}_b1': jnp.zeros((l, h), jnp.float32), f'{prefix}_w2': jax.random.normal(ks[3], (l, h, d), jnp.float32) * s_h, f'{prefix}_b2': jnp.zeros((l, d), jnp.float32)}

        def _fff(x, node_w, node_b, w1, b1, w2, b2):
            Bx, Sx, D = x.shape
            xf = x.reshape(-1, D)
            N = xf.shape[0]
            cur = jnp.zeros((N,), jnp.int32)
            for _ in range(DEPTH):
                pw = node_w[cur]
                score = jnp.einsum('nd,nd->n', xf, pw) + node_b[cur]
                cur = 2 * cur + 1 + (score >= 0).astype(jnp.int32)
            leaf = cur - N_NODES
            sel = jax.nn.one_hot(leaf, N_LEAVES, dtype=xf.dtype)
            hidden_all = jax.nn.relu(jnp.einsum('nd,ldh->lnh', xf, w1) + b1[:, None, :])
            hidden = hidden_all * sel.T[:, :, None]
            out = jnp.einsum('lnh,lho->no', hidden, w2) + sel @ b2
            return out.reshape(Bx, Sx, D)
        q = _fff(x, q_node_w, q_node_b, q_w1, q_b1, q_w2, q_b2)
        k = _fff(x, k_node_w, k_node_b, k_w1, k_b1, k_w2, k_b2)
        v = _fff(x, v_node_w, v_node_b, v_w1, v_b1, v_w2, v_b2)
        scale = 1.0 / np.sqrt(LATENT).astype(np.float32)
        attn = jax.nn.softmax(jnp.einsum('bqd,bkd->bqk', q, k) * scale, axis=-1)
        return jnp.einsum('bqk,bkd->bqd', attn, v)
    x = x + jnp.tanh(g_xattn[0]) * _L0_xattn_ref(ctx_1024, _layernorm(x, axis=-1), L0_xattn_Wq, L0_xattn_bq, L0_xattn_Wk, L0_xattn_bk, L0_xattn_Wv, L0_xattn_bv, L0_xattn_Wo, L0_xattn_bo)
    x = x + jnp.tanh(g_ffn[0]) * _L0_ffn_ref(_layernorm(x, axis=-1), L0_ffn_q_node_w, L0_ffn_q_node_b, L0_ffn_q_w1, L0_ffn_q_b1, L0_ffn_q_w2, L0_ffn_q_b2, L0_ffn_k_node_w, L0_ffn_k_node_b, L0_ffn_k_w1, L0_ffn_k_b1, L0_ffn_k_w2, L0_ffn_k_b2, L0_ffn_v_node_w, L0_ffn_v_node_b, L0_ffn_v_w1, L0_ffn_v_b1, L0_ffn_v_w2, L0_ffn_v_b2)
    return x

_drawn_inputs = setup_inputs


def setup_inputs(seed=0):
    import zlib

    import numpy as np

    out = dict(_drawn_inputs(seed))
    spreads = {'L0_xattn_bq': (0.0, 0.8),
     'L0_xattn_bk': (0.0, 0.8),
     'L0_xattn_bv': (0.0, 0.1),
     'L0_xattn_bo': (0.0, 0.1),
     'L0_ffn_q_b1': (0.0, 0.8),
     'L0_ffn_q_b2': (0.0, 0.8),
     'L0_ffn_k_b1': (0.0, 0.8),
     'L0_ffn_k_b2': (0.0, 0.8),
     'L0_ffn_v_b1': (0.0, 0.643),
     'L0_ffn_v_b2': (0.0, 0.342)}
    factors = {'L0_xattn_Wq': 8.0,
     'L0_xattn_Wk': 8.0,
     'L0_ffn_q_node_w': 3.639,
     'L0_ffn_q_node_b': 8.0,
     'L0_ffn_q_w1': 4.257,
     'L0_ffn_q_w2': 3.547,
     'L0_ffn_k_node_w': 3.59,
     'L0_ffn_k_node_b': 8.0,
     'L0_ffn_k_w1': 4.128,
     'L0_ffn_k_w2': 3.531,
     'L0_ffn_v_node_b': 3.199}
    for name, (base, spread) in spreads.items():
        noise = np.random.default_rng([zlib.crc32(name.encode()), seed]).standard_normal(out[name].shape)
        drawn = base * np.exp(spread * noise) if base else spread * noise
        out[name] = jnp.asarray(drawn.astype(out[name].dtype))
    for name, factor in factors.items():
        out[name] = (out[name] * factor).astype(out[name].dtype)
    return out
```

```python
import concourse.bass as bass
from concourse import mybir
from contextlib import ExitStack

F32 = mybir.dt.float32
BF16 = mybir.dt.bfloat16
I32 = mybir.dt.int32
ALU = mybir.AluOpType
ACT = mybir.ActivationFunctionType
AX = mybir.AxisListType

P = 128
B, S, D = 4, 512, 256
H, HD = 16, 16
TB = S // P
T = B * TB
KT = D // P
HG = 4
NG = H // HG
STRIP = 32
LEAVES, HID, DEPTH = 16, 64, 4
NODES = LEAVES - 1
SETS = 3
SLOTS = B * S // P + LEAVES - 1
EPS = 1e-5
MASKED = -1e30
Q_PARTS = [0, 0, 0, 1, 1, 2]
K_PARTS = [0, 1, 2, 0, 1, 0]
ROWS = HD * len(Q_PARTS)
ROWS_MAX = ROWS + 3
WIDTH = [S - P * j for j in range(TB)]
START = [sum(WIDTH[:j]) for j in range(TB)]
SEEN = sum(WIDTH)

MAX_UNITS = [(0, [0, 1, 2, 3]), (1, [0, 1]), (1, [2, 3])] + [(i, [h]) for i in (2, 3) for h in range(HG)]
EXP_UNITS = [(j, [h]) for j in (0, 1) for h in range(HG)] + [(2, [0, 1]), (2, [2, 3]), (3, [0, 1, 2, 3])]
NU = len(MAX_UNITS)
assert NU == len(EXP_UNITS)
MAX_BANKS, EXP_BANKS = 2, 3
PV_LAG = 3


def build(nc, x, ctxt, g_x, g_f, wq, bq, wk, bk, wv, bv, wo, bo, trees, out):
    xr = x.rearrange("b (t p) d -> b p t d", p=P)
    cr = ctxt.rearrange("b (t p) d -> b p t d", p=P)
    outr = out.rearrange("b (t p) d -> b p t d", p=P)
    parts_dram = nc.dram_tensor("parts_dram", (B, 2, 3, D, S), BF16, kind="Internal").ap()
    xs_dram = nc.dram_tensor("xs_dram", (B * S, D), F32, kind="Internal").ap()
    ys_dram = [nc.dram_tensor(f"ys_dram{s}", (SLOTS * P, D), F32, kind="Internal").ap() for s in range(SETS)]

    stack = ExitStack()
    with stack:
        def sb(name, shape, dt=F32):
            return stack.enter_context(nc.sbuf_tensor(name, shape, dt))

        def pb(name, shape, dt=F32):
            return stack.enter_context(nc.psum_tensor(name, shape, dt))

        def sem(name):
            return stack.enter_context(nc.semaphore(name))

        X = sb("X", [P, T, D])
        CX = sb("CX", [P, TB, D])
        XN = sb("XN", [P, TB, D])
        XT = sb("XT", [P, KT, S])
        CT = sb("CT", [P, KT, S])
        WQT = sb("WQT", [P, KT, D])
        WKT = sb("WKT", [P, KT, D])
        WVT = sb("WVT", [P, KT, D])
        WOT = sb("WOT", [P, NG, D])
        NODET = sb("NODET", [P, KT, SETS * NODES])
        B1T = sb("B1T", [HID, SETS * LEAVES])
        Q32 = sb("Q32", [P, 4, S])
        R1 = sb("R1", [P, 2, S])
        PARTS = sb("PARTS", [P, 4, 3, S], BF16)
        QK = sb("QK", [P, 2, 2, H * S], BF16)
        VA = sb("VA", [P, 2, TB, H, STRIP])
        PT = sb("PT", [P, 2, HG, SEEN])
        AT = sb("AT", [P, NG, S])
        DEN = sb("DEN", [P, 2, S])
        ident = sb("ident", [P, P])
        identb = sb("identb", [P, P], BF16)
        maskb = sb("maskb", [P, P], BF16)
        trib = sb("trib", [P, P], BF16)
        onesb = sb("onesb", [P, P], BF16)
        iota_row = sb("iota_row", [P, P])
        iota_part = sb("iota_part", [P, 1])
        iota_t = sb("iota_t", [P, T])
        bias = sb("bias", [P, 2, KT])
        bvb = sb("bvb", [P, D])
        nbb = sb("nbb", [P, SETS * NODES])
        gates = sb("gates", [P, 2])
        tg = sb("tg", [P, 2])
        stats = sb("stats", [P, TB, 6])
        mv = sb("mv", [P, TB, 2])
        ve = sb("ve", [P, TB])
        y0 = sb("y0", [P, TB])
        nt = sb("nt", [P, 2, TB])
        MX = sb("MX", [P, 2, NG, TB, HG])
        MR = sb("MR", [P, 2, TB, H])
        MP = sb("MP", [P, TB, 3, H], BF16)
        MT = sb("MT", [3 * H, S], BF16)
        SC = sb("SC", [P, T, SETS * NODES])

        pt0 = PT[:, 0, :, :].rearrange("p h s -> p (h s)")
        pt1 = PT[:, 1, :, :].rearrange("p h s -> p (h s)")
        RAW = [pt0[:, KT * D * n:KT * D * (n + 1)].rearrange("p (a d) -> p a d", a=KT) for n in range(4)]
        WOP = pt0[:, 4 * KT * D:4 * KT * D + KT * NG * HG * STRIP].rearrange("p (a h s c) -> p a h s c", a=KT, h=NG, s=HG)
        RAWN = pt1[0:SETS * NODES, 0:D]
        RAWB1 = pt1[0:SETS * LEAVES, D:D + HID]
        BO = pt1[:, 512:512 + KT]
        W1 = QK[:, 0, :, :].rearrange("p a n -> p (a n)").bitcast(F32)[:, 0:SETS * LEAVES * 2 * HID]
        W2 = [QK[:, 1, 0, :].bitcast(F32), QK[:, 1, 1, :].bitcast(F32), pt0[:, 0:LEAVES * D]]

        used = [0]

        def carve(region, cols, dt=F32):
            words = cols * (2 if dt == BF16 else 4) // 4
            used[0] += words
            part = region[:, used[0] - words:used[0]]
            return part if dt == F32 else part.bitcast(dt)

        vaf = VA[:, :, :, :, :].rearrange("p a t h c -> p (a t h c)")
        TS = T * SETS
        GO = carve(vaf, TS * NODES + 0, BF16).rearrange("p (n k) -> p n k", k=NODES)
        LV = [carve(vaf, TS * 2 ** d, BF16).rearrange("p (n k) -> p n k", k=2 ** d) for d in (1, 2, 3, 4)]
        CUM = [carve(vaf, TS * LEAVES, BF16) for _ in range(2)]
        RK = carve(vaf, TS * LEAVES)
        ONE16 = carve(vaf, LEAVES)
        TOT = carve(vaf, SETS * LEAVES)
        CEND = carve(vaf, SETS * LEAVES)
        BEG = carve(vaf, SETS * LEAVES)
        POSF = carve(vaf, TS)
        TOTI = carve(vaf, SETS * LEAVES, I32)
        TILEI = carve(vaf, TS, I32)
        OFFI = carve(vaf, TS, I32)
        TILEF = carve(vaf, TS)
        OFFF = carve(vaf, TS)
        IDXF = carve(vaf, SETS * 2 * SLOTS)
        LEAFF = carve(vaf, SETS * SLOTS)
        assert used[0] <= vaf.shape[1]
        used[0] = 0
        cxf = CX[:, :, :].rearrange("p t d -> p (t d)")
        POSI = carve(cxf, TS, I32)
        IDX = carve(cxf, SETS * SLOTS, I32)
        LEAFI = carve(cxf, SETS * SLOTS, I32)
        OH = PARTS[:, :, :, :].rearrange("p c n s -> p (c n s)").rearrange("p (s t n) -> p s t n", s=SETS, t=T)
        used[0] = 0
        q32f = Q32[:, :, :].rearrange("p c s -> p (c s)")
        RHS = carve(q32f, TS * 2 * SLOTS, BF16).rearrange("p (n a k) -> p n a k", a=2, k=SLOTS)
        used[0] = 0
        r1f = R1[:, :, :].rearrange("p c s -> p (c s)")
        OHT = carve(r1f, TS * SLOTS, BF16).rearrange("p (n k) -> p n k", k=SLOTS)
        LEQ = DEN[:, :, :].rearrange("p t d -> p (t d)")[:, 0:TS * SLOTS // 2].bitcast(BF16)

        NT = SETS * SLOTS
        used[0] = 0
        GX = carve(pt1, 4 * D).rearrange("p (n d) -> p n d", n=4)
        GXT = carve(pt1, 2 * D).rearrange("p (n a c) -> p n a c", n=2, a=2)
        W1S = carve(pt1, 2 * 2 * HID).rearrange("p (n d) -> p n d", n=2)
        HT = carve(pt1, 2 * P).rearrange("p (n d) -> p n d", n=2)
        YS = carve(pt1, 4 * D).rearrange("p (n d) -> p n d", n=4)
        YQK = vaf.rearrange("p (n a t d) -> p n a t d", n=2, a=2, t=TB)
        YV = AT[:, :, :].rearrange("p g s -> p (g s)").rearrange("p (n t d) -> p n t d", n=2, t=TB)
        YT = [XT, CT]
        PR = R1
        PRT = DEN
        m2 = sb("m2", [P, 2])
        negm = sb("negm", [P, 2])
        esum = sb("esum", [P, 2])
        rd = sb("rd", [P, 2, 2])

        ps_exp = pb("ps_exp", [P, EXP_BANKS, 512])
        ps_max = pb("ps_max", [P, MAX_BANKS, 512])
        ps_pv = pb("ps_pv", [P, 512])
        ps_a = pb("ps_a", [P, 512])
        ps_d = pb("ps_d", [P, 512])

        def ps_y(i):
            return ps_a if i % 2 == 0 else ps_d

        def ps_prt(n):
            return ps_pv[:, :] if n % 2 == 0 else ps_exp[:, 2, :]

        x_in = [sem(f"x_in{b}") for b in range(B)]
        c_in = [sem(f"c_in{b}") for b in range(B)]
        w_in = [sem(f"w_in{n}") for n in range(4)]
        small_in = sem("small_in")
        node_in = sem("node_in")
        consts = sem("consts")
        wop_ready = sem("wop_ready")
        tanh_done = sem("tanh_done")
        bias_done = sem("bias_done")
        a_full, a_free = sem("a_full"), sem("a_free")
        d_full, d_free = sem("d_full"), sem("d_free")
        xn_ready = sem("xn_ready")
        chain_dve, chain_act, chain_pool = sem("chain_dve"), sem("chain_act"), sem("chain_pool")
        parts_ready = sem("parts_ready")
        parts_out = [sem(f"parts_out{n}") for n in range(2)]
        qk_in = [sem(f"qk_in{n}") for n in range(2)]
        max_full, max_free = sem("max_full"), sem("max_free")
        mp_ready = sem("mp_ready")
        mt_in = [sem(f"mt_in{n}") for n in range(2)]
        exp_full, exp_free = sem("exp_full"), sem("exp_free")
        cut_done = sem("cut_done")
        pv_done = sem("pv_done")
        at_ready = sem("at_ready")
        out_done = sem("out_done")
        xs_out = [sem(f"xs_out{b}") for b in range(B)]

        w1_in = sem("w1_in")
        w2_in = [sem(f"w2_in{n}") for n in range(SETS)]
        sel_ready, rank_full, rhs_ready, idx_full, idx_ready, leaf_ready = (
            sem(n) for n in ("sel_ready", "rank_full", "rhs_ready", "idx_full", "idx_ready", "leaf_ready"))
        gx_in = [sem(f"gx_in{n}") for n in range(4)]
        xt_full, xt_free, h_full, w1_ready, ht_free, y_full, y_free = (
            sem(n) for n in ("xt_full", "xt_free", "h_full", "w1_ready", "ht_free", "y_full", "y_free"))
        y_out = [sem(f"y_out{n}") for n in range(4)]
        u_in = [sem(f"u_in{n}") for n in range(2)]
        uv_in = [sem(f"uv_in{n}") for n in range(2)]
        ta_full, ta_free, td_full, td_free = (sem(n) for n in ("ta_full", "ta_free", "td_full", "td_free"))
        s_full, s_max, s_exp, p_full, p_free, o_full, out_ready = (
            sem(n) for n in ("s_full", "s_max", "s_exp", "p_full", "p_free", "o_full", "out_ready"))

        def front(b):
            return [("a", ("xt", b, 0)), ("d", ("xt", b, 1)), ("a", ("ct", b, 0)), ("d", ("ct", b, 1)),
                    ("a", ("q", b, 0)), ("d", ("q", b, 1)), ("a", ("k", b, 0)), ("d", ("k", b, 1)),
                    ("d", ("v", b, 0)), ("d", ("v", b, 1))]

        def back(b):
            return [("d", ("o", b, 0)), ("d", ("o", b, 1)), ("a", ("x2t", b, 0)), ("d", ("x2t", b, 1)),
                    ("d", ("n", b, 0))]

        uses = [("a", ("w", 0)), ("d", ("w", 1)), ("a", ("w", 2)), ("d", ("wo", 0)), ("a", ("wo", 1)),
                ("d", ("node", 0)), ("a", ("b1", 0))]
        uses += front(0) + front(1) + [("a", ("m", 0))]
        for b in range(B):
            if b + 1 < B:
                uses += [("a", ("m", b + 1))]
            if b + 2 < B:
                uses += front(b + 2)
            uses += back(b)
        turn = {}
        for bank in "ad":
            for n, (_, what) in enumerate([u for u in uses if u[0] == bank]):
                turn[what] = n
        emptied = dict(a=a_free, d=d_free)
        filled = dict(a=a_full, d=d_full)
        bank_of = {what: bank for bank, what in uses}
        scratch = dict(a=ps_a, d=ps_d)

        def claim(pe, what):
            if turn[what]:
                pe.wait_ge(emptied[bank_of[what]], turn[what])
            return scratch[bank_of[what]]

        block = stack.enter_context(nc.Block())

        @block.sync
        def _(sp):
            sp.dma_start(X[:, 0:TB, :], xr[0]).then_inc(x_in[0], 16)
            sp.dma_start(CX[:, :, :], cr[0]).then_inc(c_in[0], 16)
            for n, w in enumerate((wq, wk, wv, wo)):
                sp.dma_start(RAW[n], w.rearrange("(a p) d -> p a d", p=P)).then_inc(w_in[n], 16)
            sp.dma_start(X[:, TB:2 * TB, :], xr[1]).then_inc(x_in[1], 16)
            sp.dma_start(X[:, 2 * TB:3 * TB, :], xr[2]).then_inc(x_in[2], 16)
            sp.dma_start(X[:, 3 * TB:4 * TB, :], xr[3]).then_inc(x_in[3], 16)

            def bounce(b):
                for c in range(4):
                    sp.wait_ge(parts_ready, 4 * b + c + 1)
                    sp.dma_start(parts_dram[b, c // 2, :, P * (c % 2):P * (c % 2 + 1), :].rearrange("n p s -> p n s"),
                                 PARTS[:, c, :, :]).then_inc(parts_out[c // 2], 16)
                if b >= 2:
                    sp.wait_ge(exp_full, NU * NG * (b - 1))
                for s, used in enumerate((Q_PARTS, K_PARTS)):
                    sp.wait_ge(parts_out[s], 32 * (b + 1))
                    for g, n in enumerate(used):
                        sp.dma_start(QK[HD * g:HD * (g + 1), b % 2, s, :].rearrange("p (h s) -> p h s", h=H),
                                     parts_dram[b, s, n].rearrange("(h p) s -> p h s", p=HD)).then_inc(qk_in[b % 2], 16)

            def load_ctx(b):
                sp.wait_ge(a_full, turn["ct", b - 1, 0] + 1)
                sp.wait_ge(d_full, turn["ct", b - 1, 1] + 1)
                sp.dma_start(CX[:, :, :], cr[b]).then_inc(c_in[b], 16)

            def load_minus_max(b):
                sp.wait_ge(a_free, turn["m", b] + 1)
                for n in range(3):
                    sp.dma_start(QK[ROWS + n:ROWS + n + 1, b % 2, 0, :].rearrange("p (h s) -> p h s", h=H),
                                 MT[H * n:H * (n + 1), :]).then_inc(mt_in[b % 2], 16)

            load_ctx(1)
            bounce(0)
            bounce(1)
            load_minus_max(0)
            for b in range(B):
                if b + 2 < B:
                    load_ctx(b + 2)
                if b + 1 < B:
                    load_minus_max(b + 1)
                if b + 2 < B:
                    bounce(b + 2)
                sp.wait_ge(xn_ready, XN2_TURN(b))
                sp.dma_start(xs_dram[S * b:S * (b + 1), :].rearrange("(t p) d -> p t d", p=P),
                             XN[:, :, :]).then_inc(xs_out[b], 16)
                if b == B - 2:
                    sp.wait_ge(exp_full, NU * NG * (B - 1))
                    for s in range(SETS):
                        sp.dma_start(W1[:, LEAVES * 2 * HID * s:LEAVES * 2 * HID * (s + 1)].rearrange("p (l n) -> p l n", l=LEAVES),
                                     trees[s][2].rearrange("l (p j) h -> p l (j h)", j=2)).then_inc(w1_in, 16)
            for s in range(SETS):
                if s == 0:
                    sp.wait_ge(exp_full, NU * NG * B)
                if s == 2:
                    sp.wait_ge(pv_done, TB * NG * B)
                sp.dma_start(W2[s][0:HID, :].rearrange("p (l d) -> p l d", l=LEAVES),
                             trees[s][4].rearrange("l h d -> h l d")).then_inc(w2_in[s], 16)
                sp.dma_start(W2[s][HID:HID + 1, :], trees[s][5].rearrange("(a l) d -> a (l d)", a=1)).then_inc(w2_in[s], 16)
            for b in range(B):
                sp.wait_ge(xs_out[b], 16)
            for i in range(NT):
                sp.wait_ge(y_free, i + 1)
                sp.dma_start(ys_dram[i // SLOTS][P * (i % SLOTS):P * (i % SLOTS + 1), :],
                             YS[:, i % 4, :]).then_inc(y_out[i % 4], 16)
            for n in range(T):
                sp.wait_ge(out_ready, n + 1)
                sp.dma_start(outr[n // TB, :, n % TB, :], X[:, n, :]).then_inc(out_done, 16)
            sp.wait_ge(out_done, 16 * T)

        @block.gpsimd
        def _(pool):
            links = 0

            def link(ins):
                nonlocal links
                links += 1
                ins.then_inc(chain_pool, 1)
                pool.wait_ge(chain_pool, links)

            made = 0

            def const(ins):
                nonlocal made
                made += 1
                ins.then_inc(consts, 1)
                pool.wait_ge(consts, made)

            def small(dst, src):
                pool.dma_start(dst, src).then_inc(small_in, 16)

            small(gates[:, 0:1], g_x.to_broadcast([P, 1]))
            small(gates[:, 1:2], g_f.to_broadcast([P, 1]))
            small(bvb[:, :], bv.rearrange("(a d) -> a d", a=1).to_broadcast([P, D]))
            for s in range(SETS):
                small(nbb[:, NODES * s:NODES * (s + 1)],
                      trees[s][1].rearrange("(a d) -> a d", a=1).to_broadcast([P, NODES]))
                pool.dma_start(RAWN[NODES * s:NODES * (s + 1), :], trees[s][0]).then_inc(node_in, 16)
                pool.dma_start(RAWB1[LEAVES * s:LEAVES * (s + 1), :], trees[s][3]).then_inc(node_in, 16)
            with nc.allow_non_contiguous_dma(reason="three vectors of 256 elements"):
                small(bias[:, 0, :], bq.rearrange("(a p) -> p a", p=P))
                small(bias[:, 1, :], bk.rearrange("(a p) -> p a", p=P))
                small(BO, bo.rearrange("(a p) -> p a", p=P))
            link(nc.gpsimd.memset(ident[:, :], 0.0))
            link(nc.gpsimd.affine_select(out=ident[:, :], in_=ident[:, :], compare_op=ALU.not_equal, fill=1.0,
                                         base=0, pattern=[[-1, P]], channel_multiplier=1))
            const(nc.gpsimd.tensor_copy(identb[:, :], ident[:, :]))
            link(nc.gpsimd.memset(maskb[:, :], 0.0))
            const(nc.gpsimd.affine_select(out=maskb[:, :], in_=maskb[:, :], compare_op=ALU.is_ge, fill=MASKED,
                                          base=0, pattern=[[-1, P]], channel_multiplier=1))
            link(nc.gpsimd.memset(WOP, 0.0))
            pool.wait_ge(w_in[3], 16)
            pool.wait_ge(small_in, 16 * SMALLS)
            for a in range(KT):
                for h in range(NG):
                    link(nc.gpsimd.tensor_copy(WOP[:, a, h, :, 0:HD],
                                               RAW[3][:, a, P // 2 * h:P // 2 * (h + 1)].rearrange("p (s c) -> p s c", s=HG)))
                last = nc.gpsimd.tensor_copy(WOP[:, a, 0, 0, HD:HD + 1], BO[:, a:a + 1])
                if a + 1 < KT:
                    link(last)
            last.then_inc(wop_ready, 1)
            pool.wait_ge(wop_ready, 1)
            for b in range(2):
                link(nc.gpsimd.memset(VA[:, b, :, :, HD:STRIP], 1.0))
            for b in range(2):
                const(nc.gpsimd.memset(QK[ROWS:ROWS + STRIP, b, 1, :], 1.0))
            link(nc.gpsimd.memset(onesb[:, :], 1.0))
            link(nc.gpsimd.affine_select(out=trib[:, :], in_=onesb[:, :], compare_op=ALU.is_gt, fill=0.0,
                                    base=0, pattern=[[1, P]], channel_multiplier=-1))
            const(nc.gpsimd.iota(iota_row[:, :], pattern=[[1, P]], base=0, channel_multiplier=0,
                           allow_small_or_imprecise_dtypes=True))
            const(nc.gpsimd.iota(iota_part[:, :], pattern=[[0, 1]], base=0, channel_multiplier=1,
                           allow_small_or_imprecise_dtypes=True))
            const(nc.gpsimd.iota(iota_t[:, :], pattern=[[1, T]], base=0, channel_multiplier=0,
                           allow_small_or_imprecise_dtypes=True))

            def split(b):
                for c in range(4):
                    bank, what = ("a", "d")[c % 2], (("q", "k")[c // 2], b, c % 2)
                    pool.wait_ge(emptied[bank], turn[what] + 1)
                    link(nc.gpsimd.tensor_tensor(R1[:, c % 2, :], Q32[:, c, :], PARTS[:, c, 0, :], ALU.subtract))
                    link(nc.gpsimd.tensor_copy(PARTS[:, c, 1, :], R1[:, c % 2, :]))
                    nc.gpsimd.tensor_tensor(PARTS[:, c, 2, :], R1[:, c % 2, :], PARTS[:, c, 1, :],
                                            ALU.subtract).then_inc(parts_ready, 1)
                    pool.wait_ge(parts_ready, 4 * b + c + 1)

            split(0)
            split(1)
            for b in range(B):
                for hg in range(NG):
                    for j in range(TB):
                        last = max(u for u, (jj, _) in enumerate(EXP_UNITS) if jj == j)
                        pool.wait_ge(exp_free, NU * (NG * b + hg) + last + 1)
                        blk = PT[:, (NG * b + hg) % 2, :, START[j]:START[j] + P]
                        nc.gpsimd.affine_select(out=blk, in_=blk, compare_op=ALU.is_ge, fill=0.0, base=0,
                                                pattern=[[0, HG], [1, P]], channel_multiplier=-1).then_inc(cut_done, 1)
                        pool.wait_ge(cut_done, TB * (NG * b + hg) + j + 1)
                if b + 2 < B:
                    split(b + 2)
            pool.wait_ge(idx_ready, 1)
            for b in range(B):
                pool.wait_ge(xs_out[b], 16)
            for i in range(NT):
                if i >= 4:
                    pool.wait_ge(xt_full, i - 3)
                nc.gpsimd.indirect_dma_start(
                    out=GX[:, i % 4, :], out_offset=None, in_=xs_dram[:, :],
                    in_offset=bass.IndirectOffsetOnAxis(ap=IDX[:, i:i + 1], axis=0)).then_inc(gx_in[i % 4], 16)
            for n in range(4):
                pool.wait_ge(y_out[n], 16 * len(range(n, NT, 4)))
            for b in range(B):
                if b >= 2:
                    pool.wait_ge(s_full, TB * (b - 1))
                    pool.wait_ge(o_full, TB * (b - 1))
                for t in range(TB):
                    for s in range(SETS):
                        dst = YQK[:, b % 2, s, t, :] if s < 2 else YV[:, b % 2, t, :]
                        c = (TB * b + t) * SETS + s
                        nc.gpsimd.indirect_dma_start(
                            out=dst, out_offset=None, in_=ys_dram[s][:, :],
                            in_offset=bass.IndirectOffsetOnAxis(ap=POSI[:, c:c + 1], axis=0)).then_inc(
                                (u_in if s < 2 else uv_in)[b % 2], 16)

        @block.scalar
        def _(act):
            act.wait_ge(small_in, 16 * SMALLS)
            nc.scalar.activation(tg[:, :], gates[:, :], ACT.Tanh).then_inc(tanh_done, 1)

            def evac(what, dst, src, func=ACT.Copy, **kw):
                act.wait_ge(a_full, turn[what] + 1)
                nc.scalar.activation(dst, src, func, **kw).then_inc(a_free, 1)

            wide = ps_a[:, :].rearrange("p (a s) -> p a s", a=KT)
            evac(("w", 0), WQT[:, :, :], wide)
            evac(("w", 2), WVT[:, :, :], wide)
            evac(("wo", 1), WOT[:, 2:4, :], wide)
            evac(("b1", 0), B1T[:, :], ps_a[0:HID, 0:SETS * LEAVES])

            def evac_parts(what, c, s):
                act.wait_ge(a_full, turn[what] + 1)
                nc.scalar.activation(Q32[:, c, :], ps_a[:, :], ACT.Identity, bias=bias[:, s, 0:1], scale=QSCALE[s])
                nc.scalar.activation(PARTS[:, c, 0, :], ps_a[:, :], ACT.Identity, bias=bias[:, s, 0:1],
                                     scale=QSCALE[s]).then_inc(a_free, 1)

            def evac_front(b):
                if b:
                    act.wait_ge(d_full, turn["k", b - 1, 1] + 1)
                    act.wait_ge(d_full, turn["v", b - 1, 1] + 1)
                evac(("xt", b, 0), XT[:, 0, :], ps_a[:, :])
                evac(("ct", b, 0), CT[:, 0, :], ps_a[:, :])
                if b == 0:
                    act.wait_ge(bias_done, 1)
                else:
                    act.wait_ge(parts_ready, 4 * b)
                    act.wait_ge(parts_out[0], 32 * b)
                    act.wait_ge(parts_out[1], 32 * b)
                evac_parts(("q", b, 0), 0, 0)
                evac_parts(("k", b, 0), 2, 1)

            def evac_minus_max(b):
                if b:
                    act.wait_ge(mt_in[(b - 1) % 2], 48 * ((b - 1) // 2 + 1))
                evac(("m", b), MT[:, :], ps_a[0:3 * H, 0:S // 2].bitcast(BF16))

            evac_front(0)
            evac_front(1)
            evac_minus_max(0)
            for b in range(B):
                for hg in range(NG):
                    grp = NG * b + hg
                    if grp >= 2:
                        act.wait_ge(pv_done, TB * (grp - 1))
                    for u, (j, heads) in enumerate(EXP_UNITS):
                        k = NU * grp + u
                        act.wait_ge(exp_full, k + 1)
                        w = WIDTH[j]
                        nc.scalar.activation(
                            PT[:, grp % 2, heads[0]:heads[-1] + 1, START[j]:START[j] + w],
                            ps_exp[:, k % EXP_BANKS, 0:w * len(heads)].rearrange("p (h s) -> p h s", h=len(heads)),
                            ACT.Exp).then_inc(exp_free, 1)
                if b + 1 < B:
                    evac_minus_max(b + 1)
                if b + 2 < B:
                    evac_front(b + 2)
                evac(("x2t", b, 0), XT[:, 0, :], ps_a[:, :])

            act.wait_ge(leaf_ready, 1)
            for i in range(NT + 1):
                if i < NT:
                    act.wait_ge(xt_full, i + 1)
                    if i >= 2:
                        act.wait_ge(h_full, i - 1)
                    nc.scalar.activation(GXT[:, i % 2, :, :], ps_exp[:, i % 2, 0:D].rearrange("p (a c) -> p a c", a=2),
                                         ACT.Copy).then_inc(xt_free, 1)
                r = i - 1
                if r >= 0:
                    leaf = nc.scalar.value_load(LEAFI[0:1, r:r + 1], min_val=0, max_val=LEAVES - 1)
                    act.wait_ge(h_full, r + 1)
                    if r >= 2:
                        act.wait_ge(y_full, r - 1)
                    nc.scalar.activation(HT[0:HID, r % 2, :], ps_max[0:HID, r % 2, 0:P], ACT.Relu,
                                         bias=B1T[:, bass.ds(leaf + LEAVES * (r // SLOTS), 1)]).then_inc(ht_free, 1)
            for n in range(T + 1):
                b = n // TB
                if n < T and n % TB == 0:
                    if b:
                        act.wait_ge(s_full, TB * b)
                    for s in range(2):
                        act.wait_ge(ta_full, 2 * b + s + 1)
                        nc.scalar.activation(YT[s][:, 0, :], ps_exp[:, 0, :], ACT.Copy).then_inc(ta_free, 1)
                if n < T:
                    act.wait_ge(s_max, n + 1)
                    if n >= 2:
                        act.wait_ge(p_full, n - 1)
                    nc.scalar.activation(PR[:, n % 2, :], ps_max[:, n % 2, :], ACT.Exp, bias=negm[:, n % 2:n % 2 + 1],
                                         scale=D ** -0.5, accum_out=esum[:, n % 2:n % 2 + 1]).then_inc(s_exp, 1)
                r = n - 1
                if r >= 0:
                    act.wait_ge(p_full, r + 1)
                    if r >= 2:
                        act.wait_ge(o_full, r - 1)
                    nc.scalar.activation(PRT[:, r % 2, :], ps_prt(r), ACT.Copy).then_inc(p_free, 1)

        @block.tensor
        def _(pe):
            pe.wait_ge(consts, 2)

            def transposes(what, srcs, idn=ident, dt=F32):
                ps = claim(pe, what)
                ps = ps[:, :] if dt == F32 else ps[:, :].bitcast(dt)
                at = 0
                for src in srcs:
                    k, m = src.shape[0], src.shape[1]
                    last = nc.tensor.transpose(ps[0:m, at:at + k], src, idn[0:k, 0:k])
                    at += k
                last.then_inc(filled[bank_of[what]], 1)

            for n in range(3):
                pe.wait_ge(w_in[n], 16)
                transposes(("w", n), [RAW[n][:, a, P * k:P * (k + 1)] for k in range(KT) for a in range(KT)])
            pe.wait_ge(wop_ready, 1)
            for n in range(2):
                transposes(("wo", n), [WOP[:, a, h, :, :].rearrange("p s c -> p (s c)")
                                       for h in (2 * n, 2 * n + 1) for a in range(KT)])
            pe.wait_ge(node_in, 96)
            transposes(("node", 0), [RAWN[:, P * k:P * (k + 1)] for k in range(KT)])
            transposes(("b1", 0), [RAWB1])

            def front_pe(b):
                pe.wait_ge(xn_ready, XN1_TURN(b))
                for k in range(KT):
                    transposes(("xt", b, k), [XN[:, t, P * k:P * (k + 1)] for t in range(TB)])
                pe.wait_ge(c_in[b], 16)
                for k in range(KT):
                    transposes(("ct", b, k), [CX[:, t, P * k:P * (k + 1)] for t in range(TB)])
                for s, (nm, wt, src, what) in enumerate((("q", WQT, XT, "xt"), ("k", WKT, CT, "ct"))):
                    for m in range(KT):
                        ps = claim(pe, (nm, b, m))
                        if m == 0:
                            pe.wait_ge(a_free, turn[what, b, 0] + 1)
                            pe.wait_ge(d_free, turn[what, b, 1] + 1)
                        for k in range(KT):
                            last = nc.tensor.matmul(ps[:, :], wt[:, k, P * m:P * (m + 1)], src[:, k, :],
                                                    start=(k == 0), stop=(k == KT - 1))
                        last.then_inc(filled[bank_of[nm, b, m]], 1)
                for u in range(2):
                    ps = claim(pe, ("v", b, u))
                    for t in range(2):
                        for k in range(KT):
                            last = nc.tensor.matmul(ps[:, D * t:D * (t + 1)],
                                                    CT[:, k, P * (2 * u + t):P * (2 * u + t + 1)], WVT[:, k, :],
                                                    start=(k == 0), stop=(k == KT - 1))
                    last.then_inc(d_full, 1)

            def q_of(b, h, rows, lo, hi):
                return QK[0:rows, b % 2, 0, S * h + lo:S * h + hi]

            def k_of(b, h, rows, lo, hi):
                return QK[0:rows, b % 2, 1, S * h + lo:S * h + hi]

            def max_unit(b, n):
                hg, (i, heads) = n // NU, MAX_UNITS[n % NU]
                k = NU * NG * b + n
                if n == 0:
                    pe.wait_ge(qk_in[b % 2], 16 * 12 * (b // 2 + 1))
                if k >= MAX_BANKS:
                    pe.wait_ge(max_free, k - MAX_BANKS + 1)
                w = P * (i + 1)
                ps = ps_max[:, k % MAX_BANKS, 0:w * len(heads)].rearrange("p (h s) -> p h s", h=len(heads))
                for a, h in enumerate(heads):
                    nc.tensor.matmul(ps[:, a, :], q_of(b, HG * hg + h, ROWS, P * i, P * (i + 1)),
                                     k_of(b, HG * hg + h, ROWS, 0, w), start=(a == 0), stop=False,
                                     skip_group_check=True)
                for a, h in enumerate(heads):
                    last = nc.tensor.matmul(ps[:, a, P * i:w], identb[:, :], maskb[:, :], start=False,
                                            stop=(a == len(heads) - 1), skip_group_check=True)
                last.then_inc(max_full, 1)

            def exp_unit(b, n):
                hg, (j, heads) = n // NU, EXP_UNITS[n % NU]
                k = NU * NG * b + n
                if n == 0:
                    pe.wait_ge(mt_in[b % 2], 48 * (b // 2 + 1))
                    pe.wait_ge(consts, 4)
                if k >= EXP_BANKS:
                    pe.wait_ge(exp_free, k - EXP_BANKS + 1)
                w = WIDTH[j]
                for a, h in enumerate(heads):
                    last = nc.tensor.matmul(ps_exp[:, k % EXP_BANKS, w * a:w * (a + 1)],
                                            k_of(b, HG * hg + h, ROWS_MAX, P * j, P * (j + 1)),
                                            q_of(b, HG * hg + h, ROWS_MAX, P * j, S), start=True, stop=True)
                last.then_inc(exp_full, 1)

            def pv(b, hg, j):
                grp = NG * b + hg
                if hg == 0 and j == 0:
                    pe.wait_ge(d_free, turn["v", b, 1] + 1)
                if j == 0 and grp:
                    pe.wait_ge(at_ready, grp)
                pe.wait_ge(cut_done, TB * grp + j + 1)
                for h in range(HG):
                    last = nc.tensor.matmul(ps_pv[STRIP * h:STRIP * (h + 1), P * j:S],
                                            VA[:, b % 2, j, HG * hg + h, :],
                                            PT[:, grp % 2, h, START[j]:START[j] + WIDTH[j]],
                                            start=(j == 0), stop=(j == TB - 1), skip_group_check=True)
                last.then_inc(pv_done, 1)

            def minus_max(b):
                pe.wait_ge(mp_ready, b + 1)
                transposes(("m", b), [MP[:, t, :, :].rearrange("p n h -> p (n h)") for t in range(TB)], identb, BF16)

            def back_pe(b):
                pe.wait_ge(at_ready, NG * (b + 1))
                for u in range(2):
                    ps = claim(pe, ("o", b, u))
                    for t in range(2):
                        for h in range(NG):
                            last = nc.tensor.matmul(ps[:, D * t:D * (t + 1)],
                                                    AT[:, h, P * (2 * u + t):P * (2 * u + t + 1)], WOT[:, h, :],
                                                    start=(h == 0), stop=(h == NG - 1))
                    last.then_inc(d_full, 1)
                pe.wait_ge(xn_ready, XN2_TURN(b))
                for k in range(KT):
                    transposes(("x2t", b, k), [XN[:, t, P * k:P * (k + 1)] for t in range(TB)])
                ps = claim(pe, ("n", b, 0))
                pe.wait_ge(a_free, turn["x2t", b, 0] + 1)
                pe.wait_ge(d_free, turn["x2t", b, 1] + 1)
                w = SETS * NODES
                for t in range(TB):
                    for k in range(KT):
                        last = nc.tensor.matmul(ps[:, w * t:w * (t + 1)], XT[:, k, P * t:P * (t + 1)], NODET[:, k, :],
                                                start=(k == 0), stop=(k == KT - 1))
                last.then_inc(d_full, 1)

            front_pe(0)
            front_pe(1)
            for n in range(NU * NG):
                max_unit(0, n)
            minus_max(0)
            for b in range(B):
                due = {}
                for hg in range(NG):
                    for j in range(TB):
                        last = max(u for u, (jj, _) in enumerate(EXP_UNITS) if jj == j)
                        due.setdefault(NU * hg + last + PV_LAG, []).append((hg, j))
                for n in range(NU * NG + PV_LAG):
                    if n < NU * NG:
                        exp_unit(b, n)
                        if b + 1 < B:
                            max_unit(b + 1, n)
                    for hg, j in due.get(n, []):
                        pv(b, hg, j)
                if b + 1 < B:
                    minus_max(b + 1)
                if b + 2 < B:
                    front_pe(b + 2)
                back_pe(b)

            pe.wait_ge(sel_ready, 1)
            w = SETS * LEAVES
            sel, cum = LV[3].rearrange("p n k -> p (n k)"), CUM[1]
            for half in range(2):
                ps = ps_exp[:, half, 0:T // 2 * w]
                nc.tensor.matmul(ps, trib[:, :], sel[:, T // 2 * w * half:T // 2 * w * (half + 1)], start=True,
                                 stop=False, skip_group_check=True)
                lo = w if half == 0 else 0
                nc.tensor.matmul(ps[:, lo:T // 2 * w], onesb[:, :],
                                 cum[:, T // 2 * w * half + lo - w:T // 2 * w * (half + 1) - w], start=False,
                                 stop=True, skip_group_check=True)
            nc.tensor.matmul(ps_exp[:, 2, 0:w], onesb[:, :], cum[:, w * (T - 1):w * T], start=True,
                             stop=True).then_inc(rank_full, 1)
            pe.wait_ge(rhs_ready, 1)
            for s in range(SETS):
                for t in range(T):
                    last = nc.tensor.matmul(ps_max[:, 0, 2 * SLOTS * s:2 * SLOTS * (s + 1)], OH[:, s, t, :],
                                            RHS[:, SETS * t + s, :, :].rearrange("p a k -> p (a k)"),
                                            start=(t == 0), stop=(t == T - 1), skip_group_check=True)
            last.then_inc(idx_full, 1)

            pe.wait_ge(w1_in, 48)
            pe.wait_ge(leaf_ready, 1)
            leaf = {}
            for i in range(NT + 2):
                if i < NT:
                    pe.wait_ge(gx_in[i % 4], 16 * (i // 4 + 1))
                    if i >= 2:
                        pe.wait_ge(xt_free, i - 1)
                    for a in range(2):
                        last = nc.tensor.transpose(ps_exp[:, i % 2, P * a:P * (a + 1)], GX[:, i % 4, a:D:2], ident[:, :])
                    last.then_inc(xt_full, 1)
                r = i - 1
                if 0 <= r < NT:
                    leaf[r] = nc.tensor.value_load(LEAFI[0:1, r:r + 1], min_val=0, max_val=LEAVES - 1)
                    pe.wait_ge(xt_free, r + 1)
                    pe.wait_ge(w1_ready, r + 1)
                    if r >= 2:
                        pe.wait_ge(ht_free, r - 1)
                    for a in range(2):
                        last = nc.tensor.matmul(ps_max[0:HID, r % 2, 0:P], W1S[:, r % 2, HID * a:HID * (a + 1)],
                                                GXT[:, r % 2, a, :], start=(a == 0), stop=(a == 1))
                    last.then_inc(h_full, 1)
                r = i - 2
                if 0 <= r < NT:
                    if r % SLOTS == 0:
                        pe.wait_ge(w2_in[r // SLOTS], 32)
                    pe.wait_ge(ht_free, r + 1)
                    if r >= 2:
                        pe.wait_ge(y_free, r - 1)
                    nc.tensor.matmul(ps_y(r)[:, 0:D], HT[0:HID + 1, r % 2, :],
                                     W2[r // SLOTS][0:HID + 1, bass.ds(leaf.pop(r) * D, D)], start=True,
                                     stop=True).then_inc(y_full, 1)

            for n in range(T + 2):
                b = n // TB
                if n < T and n % TB == 0:
                    pe.wait_ge(u_in[b % 2], 16 * 2 * TB * (b // 2 + 1))
                    for s in range(2):
                        for k in range(KT):
                            if 2 * b + s:
                                pe.wait_ge((ta_free, td_free)[k], 2 * b + s)
                            for t in range(TB):
                                last = nc.tensor.transpose(ps_exp[:, k, P * t:P * (t + 1)],
                                                           YQK[:, b % 2, s, t, P * k:P * (k + 1)], ident[:, :])
                            last.then_inc((ta_full, td_full)[k], 1)
                if n < T:
                    if n % TB == 0:
                        pe.wait_ge(ta_free, 2 * b + 2)
                        pe.wait_ge(td_free, 2 * b + 2)
                    if n >= 2:
                        pe.wait_ge(s_exp, n - 1)
                    t = n % TB
                    for k in range(KT):
                        last = nc.tensor.matmul(ps_max[:, n % 2, :], YT[0][:, k, P * t:P * (t + 1)], YT[1][:, k, :],
                                                start=(k == 0), stop=(k == KT - 1))
                    last.then_inc(s_full, 1)
                r = n - 1
                if 0 <= r < T:
                    pe.wait_ge(s_exp, r + 1)
                    if r >= 2:
                        pe.wait_ge(p_free, r - 1)
                    for k in range(TB):
                        last = nc.tensor.transpose(ps_prt(r)[:, P * k:P * (k + 1)], PR[:, r % 2, P * k:P * (k + 1)], ident[:, :])
                    last.then_inc(p_full, 1)
                r = n - 2
                if 0 <= r < T:
                    if r % TB == 0:
                        pe.wait_ge(uv_in[r // TB % 2], 16 * TB * (r // TB // 2 + 1))
                    pe.wait_ge(p_free, r + 1)
                    if r >= 2:
                        pe.wait_ge(out_ready, r - 1)
                    for k in range(TB):
                        last = nc.tensor.matmul(ps_y(r)[:, 0:D], PRT[:, r % 2, P * k:P * (k + 1)],
                                                YV[:, r // TB % 2, k, :], start=(k == 0), stop=(k == TB - 1))
                    last.then_inc(o_full, 1)

        @block.vector
        def _(dve):
            links = 0

            def link(ins):
                nonlocal links
                links += 1
                ins.then_inc(chain_dve, 1)
                dve.wait_ge(chain_dve, links)

            def layernorm(src, in_ready):
                in_ready()
                for t in range(TB):
                    last = nc.vector.bn_stats(stats[:, t, :], src[:, t, :])
                link(last)
                for t in range(TB):
                    last = nc.vector.bn_aggr(mv[:, t, :], stats[:, t, :])
                link(last)
                link(nc.vector.tensor_scalar(ve[:, :], mv[:, :, 1], EPS, None, ALU.add))
                link(nc.vector.tensor_scalar(y0[:, :].bitcast(I32), ve[:, :].bitcast(I32), 1, None,
                                             ALU.arith_shift_right))
                link(nc.vector.tensor_scalar(y0[:, :].bitcast(I32), y0[:, :].bitcast(I32), -1.0, float(0x5F3759DF),
                                             ALU.mult, ALU.add))
                for _ in range(4):
                    link(nc.vector.tensor_tensor(nt[:, 0, :], y0[:, :], y0[:, :], ALU.mult))
                    link(nc.vector.tensor_tensor(nt[:, 1, :], nt[:, 0, :], ve[:, :], ALU.mult))
                    link(nc.vector.tensor_scalar(nt[:, 0, :], nt[:, 1, :], -0.5, 1.5, ALU.mult, ALU.add))
                    link(nc.vector.tensor_tensor(y0[:, :], y0[:, :], nt[:, 0, :], ALU.mult))
                for t in range(TB):
                    last = nc.vector.tensor_scalar(XN[:, t, :], src[:, t, :], mv[:, t, 0:1], y0[:, t:t + 1],
                                                   ALU.subtract, ALU.mult)
                last.then_inc(xn_ready, 1)

            def norm_in(b):
                def ready():
                    dve.wait_ge(x_in[b], 16)
                    if b:
                        prev = ("x2t", b - 3) if b >= 3 else ("xt", b - 1)
                        dve.wait_ge(a_full, turn[(*prev, 0)] + 1)
                        dve.wait_ge(d_full, turn[(*prev, 1)] + 1)
                        if b >= 3:
                            dve.wait_ge(xs_out[b - 3], 16)
                layernorm(X[:, TB * b:TB * (b + 1), :], ready)

            def evac(what, fn):
                dve.wait_ge(d_full, turn[what] + 1)
                fn().then_inc(d_free, 1)

            def copy(dst, src):
                return lambda: nc.vector.tensor_copy(dst, src)

            wide = ps_d[:, :].rearrange("p (a s) -> p a s", a=KT)

            def evac_parts(what, c, s):
                dve.wait_ge(d_full, turn[what] + 1)
                for dst in (Q32[:, c, :], PARTS[:, c, 0, :]):
                    last = nc.vector.tensor_scalar(dst, ps_d[:, :], QSCALE[s], bias[:, s, 1:2], ALU.mult, ALU.add)
                last.then_inc(d_free, 1)

            def evac_front(b):
                if b:
                    dve.wait_ge(d_full, turn["v", b - 1, 1] + 1)
                evac(("xt", b, 1), copy(XT[:, 1, :], ps_d[:, :]))
                evac(("ct", b, 1), copy(CT[:, 1, :], ps_d[:, :]))
                if b:
                    dve.wait_ge(parts_ready, 4 * b)
                    dve.wait_ge(parts_out[0], 32 * b)
                    dve.wait_ge(parts_out[1], 32 * b)
                evac_parts(("q", b, 1), 1, 0)
                evac_parts(("k", b, 1), 3, 1)
                if b >= 2:
                    dve.wait_ge(pv_done, TB * NG * (b - 1))
                for u in range(2):
                    dve.wait_ge(d_full, turn["v", b, u] + 1)
                    for t in range(2):
                        last = nc.vector.tensor_tensor(VA[:, b % 2, 2 * u + t, :, 0:HD],
                                                       ps_d[:, D * t:D * (t + 1)].rearrange("p (h c) -> p h c", h=H),
                                                       bvb[:, :].rearrange("p (h c) -> p h c", h=H), ALU.add)
                    last.then_inc(d_free, 1)

            def take_max(b, n):
                hg, (i, heads) = n // NU, MAX_UNITS[n % NU]
                k = NU * NG * b + n
                dve.wait_ge(max_full, k + 1)
                w = P * (i + 1)
                nc.vector.tensor_reduce(MX[:, b % 2, hg, i, heads[0]:heads[-1] + 1],
                                        ps_max[:, k % MAX_BANKS, 0:w * len(heads)].rearrange("p (h s) -> p h s", h=len(heads)),
                                        AX.X, ALU.max).then_inc(max_free, 1)

            def split_max(b):
                dve.wait_ge(max_free, NU * NG * (b + 1))
                if b:
                    dve.wait_ge(a_full, turn["m", b - 1] + 1)
                mx = MX[:, b % 2, :, :, :].rearrange("p g t h -> p t g h")
                r = [MR[:, n, :, :].rearrange("p t (g h) -> p t g h", g=NG) for n in range(2)]
                m = [MP[:, :, n, :].rearrange("p t (g h) -> p t g h", g=NG) for n in range(3)]
                for t in range(TB):
                    last = nc.vector.tensor_scalar(r[0][:, t], mx[:, t], -1.0, None, ALU.mult)
                link(last)
                link(nc.vector.tensor_copy(MP[:, :, 0, :], MR[:, 0, :, :]))
                link(nc.vector.tensor_tensor(MR[:, 1, :, :], MR[:, 0, :, :], MP[:, :, 0, :], ALU.subtract))
                link(nc.vector.tensor_copy(MP[:, :, 1, :], MR[:, 1, :, :]))
                nc.vector.tensor_tensor(MP[:, :, 2, :], MR[:, 1, :, :], MP[:, :, 1, :],
                                        ALU.subtract).then_inc(mp_ready, 1)

            def normalise(b, hg):
                grp = NG * b + hg
                dve.wait_ge(pv_done, TB * (grp + 1))
                if hg == 0 and b:
                    dve.wait_ge(d_full, turn["o", b - 1, 1] + 1)
                link(nc.vector.stream_shuffle(DEN[:, 0, :], ps_pv[:, :], [HD + i % HD for i in range(STRIP)]))
                link(nc.vector.reciprocal(DEN[:, 1, :], DEN[:, 0, :]))
                nc.vector.tensor_tensor(AT[:, hg, :], ps_pv[:, :], DEN[:, 1, :], ALU.mult).then_inc(at_ready, 1)

            def evac_back(b):
                dve.wait_ge(tanh_done, 1)
                xb = X[:, TB * b:TB * (b + 1), :]
                for u in range(2):
                    evac(("o", b, u), lambda: nc.vector.scalar_tensor_tensor(
                        out=xb[:, 2 * u:2 * u + 2, :], in0=wide, scalar=tg[:, 0:1], in1=xb[:, 2 * u:2 * u + 2, :],
                        op0=ALU.mult, op1=ALU.add))

                def ready():
                    dve.wait_ge(d_free, turn["o", b, 1] + 1)
                    prev = ("xt", b + 2) if b + 2 < B else ("x2t", b - 1)
                    dve.wait_ge(a_full, turn[(*prev, 0)] + 1)
                    dve.wait_ge(d_full, turn[(*prev, 1)] + 1)
                    if b + 2 >= B:
                        dve.wait_ge(xs_out[b - 1], 16)
                layernorm(xb, ready)
                evac(("x2t", b, 1), copy(XT[:, 1, :], ps_d[:, :]))
                w = SETS * NODES
                dve.wait_ge(d_full, turn["n", b, 0] + 1)
                for t in range(TB):
                    last = nc.vector.tensor_tensor(SC[:, TB * b + t, :], ps_d[:, w * t:w * (t + 1)], nbb[:, :], ALU.add)
                last.then_inc(d_free, 1)

            dve.wait_ge(small_in, 16 * SMALLS)
            nc.vector.tensor_scalar(bias[:, 0, :], bias[:, 0, :], QSCALE[0], None, ALU.mult).then_inc(bias_done, 1)
            dve.wait_ge(bias_done, 1)
            norm_in(0)
            evac(("w", 1), copy(WKT[:, :, :], wide))
            evac(("wo", 0), copy(WOT[:, 0:2, :], wide))
            evac(("node", 0), copy(NODET[:, :, :], ps_d[:, 0:KT * SETS * NODES].rearrange("p (a s) -> p a s", a=KT)))
            evac_front(0)
            norm_in(1)
            evac_front(1)
            for k in range(NU * NG):
                take_max(0, k)
            split_max(0)
            for b in range(B):
                if b + 2 < B:
                    norm_in(b + 2)
                for k in range(NU * NG + PV_LAG):
                    if k < NU * NG and b + 1 < B:
                        take_max(b + 1, k)
                    if k >= NU and (k - PV_LAG) % NU == 0:
                        normalise(b, (k - PV_LAG) // NU - 1)
                if b + 1 < B:
                    split_max(b + 1)
                if b + 2 < B:
                    evac_front(b + 2)
                normalise(b, NG - 1)
                evac_back(b)

            def fin_row(r):
                dve.wait_ge(o_full, r + 1)
                nc.vector.scalar_tensor_tensor(out=X[:, r, :], in0=ps_y(r)[:, 0:D], scalar=rd[:, r % 2, 1:2],
                                               in1=X[:, r, :], op0=ALU.mult, op1=ALU.add).then_inc(out_ready, 1)

            link(nc.vector.memset(ONE16, 1.0))
            link(nc.vector.memset(HT[HID:HID + 1, :, :], 1.0))
            go = SC[:, :, :].rearrange("p t n -> p (t n)")
            link(nc.vector.tensor_scalar(GO.rearrange("p n k -> p (n k)"), go, 0.0, None, ALU.is_ge))
            link(nc.vector.tensor_copy(LV[0][:, :, 1], GO[:, :, 0]))
            link(nc.vector.tensor_scalar(LV[0][:, :, 0], GO[:, :, 0], -1.0, 1.0, ALU.mult, ALU.add))
            for d in range(1, DEPTH):
                child = LV[d].rearrange("p n (k c) -> p n k c", c=2)
                link(nc.vector.tensor_tensor(child[:, :, :, 1], LV[d - 1], GO[:, :, 2 ** d - 1:2 ** (d + 1) - 1], ALU.mult))
                link(nc.vector.tensor_tensor(child[:, :, :, 0], LV[d - 1], child[:, :, :, 1], ALU.subtract))
            sel = LV[3].rearrange("p n k -> p (n k)")
            w = SETS * LEAVES
            src = sel
            for d in range(DEPTH):
                dst, m = CUM[d % 2], w * 2 ** d
                nc.vector.tensor_copy(dst[:, 0:m], src[:, 0:m])
                last = nc.vector.tensor_tensor(dst[:, m:], src[:, m:], src[:, 0:T * w - m], ALU.add)
                if d == DEPTH - 1:
                    last.then_inc(sel_ready, 1)
                else:
                    link(last)
                src = dst
            dve.wait_ge(rank_full, 1)
            link(nc.vector.tensor_scalar(TOTI, ps_exp[:, 2, 0:w], P - 1.0, None, ALU.add))
            link(nc.vector.tensor_scalar(TOTI, TOTI, P.bit_length() - 1, None, ALU.arith_shift_right))
            link(nc.vector.tensor_copy(TOT, TOTI))
            for s in range(SETS):
                lo, hi = LEAVES * s, LEAVES * (s + 1)
                last = nc.vector.tensor_tensor_scan(CEND[:, lo:hi], ONE16, TOT[:, lo:hi], 0.0, ALU.mult, ALU.add)
            link(last)
            link(nc.vector.tensor_tensor(BEG, CEND, TOT, ALU.subtract))
            for half in range(2):
                last = nc.vector.scalar_tensor_tensor(
                    out=RK.rearrange("p (t n) -> p t n", t=T)[:, T // 2 * half:T // 2 * (half + 1), :],
                    in0=BEG.unsqueeze(1).to_broadcast([P, T // 2, w]), scalar=float(P),
                    in1=ps_exp[:, half, 0:T // 2 * w].rearrange("p (t n) -> p t n", n=w), op0=ALU.mult, op1=ALU.add)
            link(last)
            link(nc.vector.tensor_tensor(RK, RK, sel, ALU.mult))
            link(nc.vector.tensor_reduce(POSF, RK.rearrange("p (n k) -> p n k", k=LEAVES), AX.X, ALU.add))
            link(nc.vector.tensor_copy(POSI, POSF))
            nc.vector.tensor_scalar(TILEI, POSI, P.bit_length() - 1, None, ALU.arith_shift_right)
            link(nc.vector.tensor_scalar(OFFI, POSI, P - 1, None, ALU.bitwise_and))
            nc.vector.tensor_copy(TILEF, TILEI)
            link(nc.vector.tensor_copy(OFFF, OFFI))
            link(nc.vector.tensor_tensor(OHT, iota_row[:, 0:SLOTS].unsqueeze(1).to_broadcast([P, TS, SLOTS]),
                                         TILEF.unsqueeze(2).to_broadcast([P, TS, SLOTS]), ALU.is_equal))
            nc.vector.tensor_tensor(RHS.rearrange("p (t s) a k -> p t s a k", t=T)[:, :, :, 0, :].rearrange("p t s k -> p t s k"),
                                    OHT.rearrange("p (t s) k -> p t s k", t=T),
                                    iota_t[:, :].unsqueeze(2).unsqueeze(3).to_broadcast([P, T, SETS, SLOTS]), ALU.mult)
            nc.vector.tensor_scalar(RHS[:, :, 1, :], OHT, iota_part[:, 0:1], None, ALU.mult)
            offs = OFFF.rearrange("p (t s) -> p t s", t=T)
            for s in range(SETS):
                last = nc.vector.tensor_tensor(OH[:, s, :, :], iota_row[:, :].unsqueeze(1).to_broadcast([P, T, P]),
                                               offs[:, :, s].unsqueeze(2).to_broadcast([P, T, P]), ALU.is_equal)
            last.then_inc(rhs_ready, 1)
            leq = LEQ.rearrange("p (s n k) -> p s n k", s=SETS, n=SLOTS)
            for s in range(SETS):
                last = nc.vector.tensor_tensor(
                    leq[:, s], CEND[:, LEAVES * s:LEAVES * (s + 1)].unsqueeze(1).to_broadcast([P, SLOTS, LEAVES]),
                    iota_row[:, 0:SLOTS].unsqueeze(2).to_broadcast([P, SLOTS, LEAVES]), ALU.is_le)
            link(last)
            link(nc.vector.tensor_reduce(LEAFF, LEQ.rearrange("p (n k) -> p n k", k=LEAVES), AX.X, ALU.add))
            nc.vector.tensor_scalar(LEAFI, LEAFF, LEAVES - 1.0, None, ALU.min).then_inc(leaf_ready, 1)
            dve.wait_ge(idx_full, 1)
            link(nc.vector.tensor_copy(IDXF, ps_max[:, 0, 0:SETS * 2 * SLOTS]))
            idxf = IDXF.rearrange("p (s a k) -> p s a k", s=SETS, a=2)
            nc.vector.scalar_tensor_tensor(out=IDX.rearrange("p (s k) -> p s k", s=SETS), in0=idxf[:, :, 0, :],
                                           scalar=float(P), in1=idxf[:, :, 1, :], op0=ALU.mult,
                                           op1=ALU.add).then_inc(idx_ready, 1)

            dve.wait_ge(leaf_ready, 1)
            dve.wait_ge(w1_in, 48)
            for i in range(NT + 2):
                if i < NT:
                    leaf = nc.vector.value_load(LEAFI[0:1, i:i + 1], min_val=0, max_val=LEAVES - 1)
                    if i >= 2:
                        dve.wait_ge(h_full, i - 1)
                    nc.vector.tensor_copy(W1S[:, i % 2, :],
                                          W1[:, bass.ds(leaf * (2 * HID) + LEAVES * 2 * HID * (i // SLOTS), 2 * HID)]
                                          ).then_inc(w1_ready, 1)
                r = i - 2
                if 0 <= r < NT:
                    dve.wait_ge(y_full, r + 1)
                    if r >= 4:
                        dve.wait_ge(y_out[r % 4], 16 * (r // 4))
                    nc.vector.tensor_copy(YS[:, r % 4, :], ps_y(r)[:, 0:D]).then_inc(y_free, 1)
            for n in range(T + 2):
                b = n // TB
                if n < T and n % TB == 0:
                    if b:
                        dve.wait_ge(s_full, TB * b)
                    for s in range(2):
                        dve.wait_ge(td_full, 2 * b + s + 1)
                        nc.vector.tensor_copy(YT[s][:, 1, :], ps_exp[:, 1, :]).then_inc(td_free, 1)
                if n < T:
                    dve.wait_ge(s_full, n + 1)
                    link(nc.vector.tensor_reduce(m2[:, n % 2:n % 2 + 1], ps_max[:, n % 2, :], AX.X, ALU.max))
                    nc.vector.tensor_scalar(negm[:, n % 2:n % 2 + 1], m2[:, n % 2:n % 2 + 1], -(D ** -0.5), None,
                                            ALU.mult).then_inc(s_max, 1)
                r = n - 1
                if 0 <= r < T:
                    dve.wait_ge(s_exp, r + 1)
                    link(nc.vector.reciprocal(rd[:, r % 2, 0:1], esum[:, r % 2:r % 2 + 1]))
                    link(nc.vector.tensor_tensor(rd[:, r % 2, 1:2], rd[:, r % 2, 0:1], tg[:, 1:2], ALU.mult))
                    if r:
                        fin_row(r - 1)
            fin_row(T - 1)


QSCALE = [HD ** -0.5, 1.0]
SMALLS = 6 + 3


def XN1_TURN(b):
    return [1, 2, 3, 5][b]


def XN2_TURN(b):
    return [4, 6, 7, 8][b]


_INS = (["x", "ctx_1024", "g_xattn", "g_ffn"]
        + [f"L0_xattn_{n}" for n in ("Wq", "bq", "Wk", "bk", "Wv", "bv", "Wo", "bo")]
        + [f"L0_ffn_{t}_{n}" for t in "qkv" for n in ("node_w", "node_b", "w1", "b1", "w2", "b2")])


def kernel(**inputs):
    import numpy as _np
    import concourse.bacc as _bacc
    from concourse import mybir as _mybir
    from concourse.bass_utils import run_bass_kernel_spmd as _run

    nc = _bacc.Bacc("TRN2", target_bir_lowering=False, num_devices=1)
    arrays, args = {}, []
    for name in _INS:
        a = _np.ascontiguousarray(inputs[name])
        arrays[f"in_{name}_dram"] = a
        args.append(nc.dram_tensor(f"in_{name}_dram", a.shape, _mybir.dt.from_np(a.dtype), kind="ExternalInput").ap())
    out = nc.dram_tensor("out_dram", (B, S, D), _mybir.dt.float32, kind="ExternalOutput").ap()
    trees = [args[12 + 6 * s:18 + 6 * s] for s in range(SETS)]
    build(nc, *args[:12], trees, out)
    r = _run(nc, [arrays], core_ids=[0])
    return r.results[0]["out_dram"]
```
